# Optimizing a Trainium2 kernel written in Bass

```python
import numpy as np
import jax
import jax.numpy as jnp

def _softmax(x, axis=-1):
    return jax.nn.softmax(x, axis=axis)

def _gelu(x):
    return jax.nn.gelu(x, approximate=True)

def _silu(x):
    return jax.nn.silu(x)

def _sigmoid(x):
    return jax.nn.sigmoid(x)

def _layernorm(x, axis=-1, eps=1e-05):
    m = jnp.mean(x, axis=axis, keepdims=True)
    v = jnp.var(x, axis=axis, keepdims=True)
    return (x - m) / jnp.sqrt(v + eps)

def _scatter_add(tgt, idx, src, axis=0):
    return tgt.at[idx].add(src)

def _segment_sum(src, seg, n):
    return jax.ops.segment_sum(src, seg, n)
kernel_name = 'mk_gnn_resnorm_d4_gnn_r32_aeb471'

def setup_inputs(seed: int=0):
    np.random.seed(seed)
    _w = jnp.asarray

    def _rec_inputs():
        import jax
        import jax.numpy as jnp
        _gk = jax.random.key(seed)
        x = -0.0003713 + 1 * jax.random.normal(jax.random.fold_in(_gk, 1), (3125, 128), jnp.float32)
        src = jax.random.randint(jax.random.fold_in(_gk, 2), (100000,), 0, 3125, jnp.int32)
        dst = jnp.minimum((3125 * jax.random.uniform(jax.random.fold_in(_gk, 3), (100000,)) ** 2.0).astype(jnp.int32), 99999)
        _o = jnp.argsort(dst, stable=True)
        src = src[_o]
        dst = dst[_o]
        edge_attr_3 = -0.000451519 + 1.00018 * jax.random.normal(jax.random.fold_in(_gk, 12), (100000, 3), jnp.float32)
        edge_weight = jax.random.uniform(jax.random.fold_in(_gk, 14), (100000,), jnp.float32, 0.0, 0.999998)
        return (x, src, dst, edge_attr_3, edge_weight)
    x, src, dst, edge_attr_3, edge_weight = _rec_inputs()

    def _L0_gnn_setup():
        import jax, jax.numpy as jnp
        import numpy as np
        N_NODES = 3125
        N_EDGES = 50000
        IN_DIM = 128
        OUT_DIM = 128
        NEG_SLOPE = 0.2
        key = jax.random.key(seed)
        k1, k2, k3, k4, k5, k6 = jax.random.split(key, 6)
        h = jax.random.normal(k1, (N_NODES, IN_DIM), dtype=jnp.float32)
        W = jax.random.normal(k2, (OUT_DIM, IN_DIM), dtype=jnp.float32) / np.sqrt(IN_DIM)
        a_s = jax.random.normal(k3, (OUT_DIM,), dtype=jnp.float32) * 0.1
        a_d = jax.random.normal(k4, (OUT_DIM,), dtype=jnp.float32) * 0.1
        src = jax.random.randint(k5, (N_EDGES,), 0, N_NODES, dtype=jnp.int64)
        dst = jax.random.randint(k6, (N_EDGES,), 0, N_NODES, dtype=jnp.int64)
        return {'h': h, 'W': W, 'a_s': a_s, 'a_d': a_d, 'src': src, 'dst': dst}
    _L0_gnn_all = _L0_gnn_setup()
    _L0_gnn_in = {k: v for k, v in _L0_gnn_all.items() if k in ('W', 'a_s', 'a_d')}
    del _L0_gnn_all

    def _L1_gnn_setup():
        import jax, jax.numpy as jnp
        import numpy as np
        N = 50000
        E = 25000
        MUL = 32
        NB = 8
        R_MAX = 1.0
        AVG = 16.0
        SQ3 = 3.0 ** 0.5

        def _radial_embedding(r):
            x = jnp.clip(r / R_MAX, 0.0, 1.0)
            centers = jnp.arange(NB, dtype=jnp.float32) / (NB - 1)
            sigma = 1.0 / (NB - 1)
            emb = jnp.exp(-0.5 * ((x[:, None] - centers[None, :]) / sigma) ** 2)
            emb = emb * NB ** 0.5 * (r <= R_MAX).astype(jnp.float32)[:, None]
            return emb
        key = jax.random.key(seed)
        k = jax.random.split(key, 12)
        inp = {'node_feats': jax.random.normal(k[0], (N, 4 * MUL), dtype=jnp.float32), 'edge_vec': jax.random.normal(k[1], (E, 3), dtype=jnp.float32), 'edge_length': jax.random.uniform(k[2], (E,), dtype=jnp.float32), 'senders': jax.random.randint(k[3], (E,), 0, N, dtype=jnp.int32), 'receivers': jax.random.randint(k[4], (E,), 0, N, dtype=jnp.int32), 'num_nodes': N, 'W_up0': jax.random.normal(k[5], (MUL, MUL), dtype=jnp.float32), 'W_up1': jax.random.normal(k[6], (MUL, MUL), dtype=jnp.float32), 'mlp_w0': jax.random.normal(k[7], (NB, 64), dtype=jnp.float32) / NB ** 0.5, 'mlp_b0': jnp.zeros((64,), dtype=jnp.float32), 'mlp_w1': jax.random.normal(k[8], (64, 64), dtype=jnp.float32) / 8.0, 'mlp_b1': jnp.zeros((64,), dtype=jnp.float32), 'mlp_w2': jax.random.normal(k[9], (64, 4 * MUL), dtype=jnp.float32) / 8.0, 'mlp_b2': jnp.zeros((4 * MUL,), dtype=jnp.float32), 'W_out0': jax.random.normal(k[10], (2 * MUL, MUL), dtype=jnp.float32), 'W_out1': jax.random.normal(k[11], (2 * MUL, MUL), dtype=jnp.float32)}
        return inp
    _L1_gnn_all = _L1_gnn_setup()
    _L1_gnn_in = {k: v for k, v in _L1_gnn_all.items() if k in ('W_up0', 'W_up1', 'mlp_w0', 'mlp_b0', 'mlp_w1', 'mlp_b1', 'mlp_w2', 'mlp_b2', 'W_out0', 'W_out1')}
    del _L1_gnn_all

    def _L2_gnn_setup():
        import jax, jax.numpy as jnp
        import numpy as np
        N_NODES = 3125
        LN_EPS = 1e-05

        def _sage_block(x, edge_index, W_l, b_l, W_r, ln_gamma, ln_beta):
            src, dst = (edge_index[0], edge_index[1])
            msg = x[src]
            agg = jax.ops.segment_sum(msg, dst, num_segments=N_NODES)
            cnt = jax.ops.segment_sum(jnp.ones_like(dst, dtype=x.dtype), dst, num_segments=N_NODES)
            agg = agg / jnp.maximum(cnt, 1.0)[:, None]
            f = agg @ W_l.T + b_l + x @ W_r.T
            f = jax.nn.gelu(f, approximate=False)
            mu = jnp.mean(f, axis=-1, keepdims=True)
            var = jnp.var(f, axis=-1, keepdims=True)
            f = (f - mu) * jax.lax.rsqrt(var + LN_EPS) * ln_gamma + ln_beta
            return f + x
        key = jax.random.key(seed)
        ks = jax.random.split(key, 5)
        d = 128
        E = 50000
        x = jax.random.normal(ks[0], (N_NODES, d), dtype=jnp.float32)
        edge_index = jax.random.randint(ks[1], (2, E), 0, N_NODES, dtype=jnp.int64)
        W_l = jax.random.normal(ks[2], (d, d), dtype=jnp.float32) / jnp.sqrt(d).astype(jnp.float32)
        b_l = jnp.zeros((d,), dtype=jnp.float32)
        W_r = jax.random.normal(ks[3], (d, d), dtype=jnp.float32) / jnp.sqrt(d).astype(jnp.float32)
        ln_gamma = jnp.ones((d,), dtype=jnp.float32)
        ln_beta = jnp.zeros((d,), dtype=jnp.float32)
        return {'x': x, 'edge_index': edge_index, 'W_l': W_l, 'b_l': b_l, 'W_r': W_r, 'ln_gamma': ln_gamma, 'ln_beta': ln_beta}
    _L2_gnn_all = _L2_gnn_setup()
    _L2_gnn_in = {k: v for k, v in _L2_gnn_all.items() if k in ('W_l', 'b_l', 'W_r', 'ln_gamma', 'ln_beta')}
    del _L2_gnn_all

    def _L3_gnn_setup():
        import jax, jax.numpy as jnp
        import numpy as np
        N_NODES = 3125
        HIDDEN = 128
        IN_FEAT = 128
        N_EDGES = 18750

        def _gcn_conv(x, W, b, row, col, norm, n_nodes):
            h = x @ W
            msg = h[row] * norm[:, None]
            agg = jax.ops.segment_sum(msg, col, num_segments=n_nodes)
            return agg + b
        key = jax.random.key(seed)
        ks = jax.random.split(key, 8)
        x = jax.random.normal(ks[0], (N_NODES, IN_FEAT), dtype=jnp.float32)
        edge_index = jax.random.randint(ks[1], (2, N_EDGES), 0, N_NODES, dtype=jnp.int64)
        s_in = 1.0 / np.sqrt(IN_FEAT)
        s_h = 1.0 / np.sqrt(HIDDEN)
        W1 = jax.random.normal(ks[2], (IN_FEAT, HIDDEN), dtype=jnp.float32) * s_in
        b1 = jnp.zeros((HIDDEN,), dtype=jnp.float32)
        W2 = jax.random.normal(ks[3], (HIDDEN, HIDDEN), dtype=jnp.float32) * s_h
        b2 = jnp.zeros((HIDDEN,), dtype=jnp.float32)
        W3 = jax.random.normal(ks[4], (HIDDEN, HIDDEN), dtype=jnp.float32) * s_h
        b3 = jnp.zeros((HIDDEN,), dtype=jnp.float32)
        return {'x': x, 'W1': W1, 'b1': b1, 'W2': W2, 'b2': b2, 'W3': W3, 'b3': b3, 'edge_index': edge_index}
    _L3_gnn_all = _L3_gnn_setup()
    _L3_gnn_in = {k: v for k, v in _L3_gnn_all.items() if k in ('W1', 'b1', 'W2', 'b2', 'W3', 'b3')}
    del _L3_gnn_all
    return {'x': x, 'src': src, 'dst': dst, 'edge_attr_3': edge_attr_3, 'edge_weight': edge_weight, 'L0_gnn_W': _L0_gnn_in['W'], 'L0_gnn_a_s': _L0_gnn_in['a_s'], 'L0_gnn_a_d': _L0_gnn_in['a_d'], 'L1_gnn_W_up0': _L1_gnn_in['W_up0'], 'L1_gnn_W_up1': _L1_gnn_in['W_up1'], 'L1_gnn_mlp_w0': _L1_gnn_in['mlp_w0'], 'L1_gnn_mlp_b0': _L1_gnn_in['mlp_b0'], 'L1_gnn_mlp_w1': _L1_gnn_in['mlp_w1'], 'L1_gnn_mlp_b1': _L1_gnn_in['mlp_b1'], 'L1_gnn_mlp_w2': _L1_gnn_in['mlp_w2'], 'L1_gnn_mlp_b2': _L1_gnn_in['mlp_b2'], 'L1_gnn_W_out0': _L1_gnn_in['W_out0'], 'L1_gnn_W_out1': _L1_gnn_in['W_out1'], 'L2_gnn_W_l': _L2_gnn_in['W_l'], 'L2_gnn_b_l': _L2_gnn_in['b_l'], 'L2_gnn_W_r': _L2_gnn_in['W_r'], 'L2_gnn_ln_gamma': _L2_gnn_in['ln_gamma'], 'L2_gnn_ln_beta': _L2_gnn_in['ln_beta'], 'L3_gnn_W1': _L3_gnn_in['W1'], 'L3_gnn_b1': _L3_gnn_in['b1'], 'L3_gnn_W2': _L3_gnn_in['W2'], 'L3_gnn_b2': _L3_gnn_in['b2'], 'L3_gnn_W3': _L3_gnn_in['W3'], 'L3_gnn_b3': _L3_gnn_in['b3']}

def reference(x, src, dst, edge_attr_3, edge_weight, L0_gnn_W, L0_gnn_a_s, L0_gnn_a_d, L1_gnn_W_up0, L1_gnn_W_up1, L1_gnn_mlp_w0, L1_gnn_mlp_b0, L1_gnn_mlp_w1, L1_gnn_mlp_b1, L1_gnn_mlp_w2, L1_gnn_mlp_b2, L1_gnn_W_out0, L1_gnn_W_out1, L2_gnn_W_l, L2_gnn_b_l, L2_gnn_W_r, L2_gnn_ln_gamma, L2_gnn_ln_beta, L3_gnn_W1, L3_gnn_b1, L3_gnn_W2, L3_gnn_b2, L3_gnn_W3, L3_gnn_b3):
    import jax
    import jax.numpy as jnp

    def _L0_gnn_ref(h, W, a_s, a_d, src, dst):
        import jax, jax.numpy as jnp
        import numpy as np
        N_NODES = 3125
        N_EDGES = 50000
        IN_DIM = 128
        OUT_DIM = 128
        NEG_SLOPE = 0.2
        z = h @ W.T
        es = z @ a_s
        ed = z @ a_d
        e = jax.nn.leaky_relu(es[src] + ed[dst], negative_slope=NEG_SLOPE)
        emax = jax.ops.segment_max(e, dst, num_segments=N_NODES)
        w = jnp.exp(e - emax[dst])
        denom = jax.ops.segment_sum(w, dst, num_segments=N_NODES)
        a = w / denom[dst]
        msgs = z[src] * a[:, None]
        out = jax.ops.segment_sum(msgs, dst, num_segments=N_NODES)
        return out

    def _L1_gnn_ref(node_feats, edge_vec, edge_length, senders, receivers, num_nodes, W_up0, W_up1, mlp_w0, mlp_b0, mlp_w1, mlp_b1, mlp_w2, mlp_b2, W_out0, W_out1):
        import jax, jax.numpy as jnp
        import numpy as np
        N = 50000
        E = 25000
        MUL = 32
        NB = 8
        R_MAX = 1.0
        AVG = 16.0
        SQ3 = 3.0 ** 0.5

        def _radial_embedding(r):
            x = jnp.clip(r / R_MAX, 0.0, 1.0)
            centers = jnp.arange(NB, dtype=jnp.float32) / (NB - 1)
            sigma = 1.0 / (NB - 1)
            emb = jnp.exp(-0.5 * ((x[:, None] - centers[None, :]) / sigma) ** 2)
            emb = emb * NB ** 0.5 * (r <= R_MAX).astype(jnp.float32)[:, None]
            return emb
        f32 = jnp.float32
        rhat = edge_vec / (jnp.linalg.norm(edge_vec, axis=-1, keepdims=True) + 1e-12)
        Y1 = SQ3 * rhat
        emb = _radial_embedding(edge_length)
        h = jax.nn.silu(emb @ mlp_w0 + mlp_b0)
        h = jax.nn.silu(h @ mlp_w1 + mlp_b1)
        w = (h @ mlp_w2 + mlp_b2).reshape(-1, 4, MUL)
        s = node_feats[:, :MUL]
        v = node_feats[:, MUL:].reshape(-1, MUL, 3)
        xs = s @ W_up0 / f32(MUL) ** 0.5
        xv = jnp.einsum('nmc,mk->nkc', v, W_up1) / f32(MUL) ** 0.5
        ss = xs[senders]
        vv = xv[senders]
        m0 = w[:, 0] * ss
        m1 = w[:, 1][:, :, None] * ss[:, :, None] * Y1[:, None, :]
        m2 = w[:, 2][:, :, None] * vv
        m3 = w[:, 3] * (jnp.einsum('emc,ec->em', vv, Y1) / SQ3)
        mid_s = jnp.concatenate([m0, m3], axis=1)
        mid_v = jnp.concatenate([m1, m2], axis=1)
        msg_s = jax.ops.segment_sum(mid_s, receivers, num_segments=num_nodes)
        msg_v = jax.ops.segment_sum(mid_v, receivers, num_segments=num_nodes)
        out_s = msg_s @ W_out0 / f32(2 * MUL) ** 0.5
        out_v = jnp.einsum('nmc,mk->nkc', msg_v, W_out1) / f32(2 * MUL) ** 0.5
        out = jnp.concatenate([out_s, out_v.reshape(-1, 3 * MUL)], axis=1)
        return out / max(AVG, 1e-08)

    def _L2_gnn_ref(x, edge_index, W_l, b_l, W_r, ln_gamma, ln_beta):
        import jax, jax.numpy as jnp
        import numpy as np
        N_NODES = 3125
        LN_EPS = 1e-05

        def _sage_block(x, edge_index, W_l, b_l, W_r, ln_gamma, ln_beta):
            src, dst = (edge_index[0], edge_index[1])
            msg = x[src]
            agg = jax.ops.segment_sum(msg, dst, num_segments=N_NODES)
            cnt = jax.ops.segment_sum(jnp.ones_like(dst, dtype=x.dtype), dst, num_segments=N_NODES)
            agg = agg / jnp.maximum(cnt, 1.0)[:, None]
            f = agg @ W_l.T + b_l + x @ W_r.T
            f = jax.nn.gelu(f, approximate=False)
            mu = jnp.mean(f, axis=-1, keepdims=True)
            var = jnp.var(f, axis=-1, keepdims=True)
            f = (f - mu) * jax.lax.rsqrt(var + LN_EPS) * ln_gamma + ln_beta
            return f + x
        return _sage_block(x, edge_index, W_l, b_l, W_r, ln_gamma, ln_beta)

    def _L3_gnn_ref(x, W1, b1, W2, b2, W3, b3, edge_index):
        import jax, jax.numpy as jnp
        import numpy as np
        N_NODES = 3125
        HIDDEN = 128
        IN_FEAT = 128
        N_EDGES = 18750

        def _gcn_conv(x, W, b, row, col, norm, n_nodes):
            h = x @ W
            msg = h[row] * norm[:, None]
            agg = jax.ops.segment_sum(msg, col, num_segments=n_nodes)
            return agg + b
        row, col = (edge_index[0], edge_index[1])
        deg = jax.ops.segment_sum(jnp.ones(row.shape[0], dtype=x.dtype), col, num_segments=N_NODES)
        deg_inv_sqrt = jnp.where(deg > 0, jax.lax.rsqrt(jnp.maximum(deg, 1.0)), 0.0)
        norm = deg_inv_sqrt[row] * deg_inv_sqrt[col]
        h = _gcn_conv(x, W1, b1, row, col, norm, N_NODES)
        h = jax.nn.relu(h)
        h = _gcn_conv(h, W2, b2, row, col, norm, N_NODES)
        h = jax.nn.relu(h)
        h = _gcn_conv(h, W3, b3, row, col, norm, N_NODES)
        return h
    edge_index = jnp.stack([src, dst])
    x = _layernorm(x + _L0_gnn_ref(x, L0_gnn_W, L0_gnn_a_s, L0_gnn_a_d, src, dst), axis=-1)
    x = _layernorm(x + _L1_gnn_ref(x, edge_attr_3, edge_weight, src, dst, 3125, L1_gnn_W_up0, L1_gnn_W_up1, L1_gnn_mlp_w0, L1_gnn_mlp_b0, L1_gnn_mlp_w1, L1_gnn_mlp_b1, L1_gnn_mlp_w2, L1_gnn_mlp_b2, L1_gnn_W_out0, L1_gnn_W_out1), axis=-1)
    x = _layernorm(x + _L2_gnn_ref(x, edge_index, L2_gnn_W_l, L2_gnn_b_l, L2_gnn_W_r, L2_gnn_ln_gamma, L2_gnn_ln_beta), axis=-1)
    x = _layernorm(x + _L3_gnn_ref(x, L3_gnn_W1, L3_gnn_b1, L3_gnn_W2, L3_gnn_b2, L3_gnn_W3, L3_gnn_b3, edge_index), axis=-1)
    return x

_drawn_inputs = setup_inputs


def setup_inputs(seed=0):
    import zlib

    import numpy as np

    out = dict(_drawn_inputs(seed))
    spreads = {'L1_gnn_mlp_b0': (0.0, 0.576),
     'L1_gnn_mlp_b1': (0.0, 0.347),
     'L1_gnn_mlp_b2': (0.0, 0.1),
     'L2_gnn_b_l': (0.0, 0.1),
     'L2_gnn_ln_gamma': (1.0, 0.2),
     'L2_gnn_ln_beta': (0.0, 0.1),
     'L3_gnn_b1': (0.0, 0.1),
     'L3_gnn_b2': (0.0, 0.1),
     'L3_gnn_b3': (0.0, 0.1)}
    factors = {}
    for name, (base, spread) in spreads.items():
        noise = np.random.default_rng([zlib.crc32(name.encode()), seed]).standard_normal(out[name].shape)
        drawn = base * np.exp(spread * noise) if base else spread * noise
        out[name] = jnp.asarray(drawn.astype(out[name].dtype))
    for name, factor in factors.items():
        out[name] = (out[name] * factor).astype(out[name].dtype)
    return out
```

```python
from contextlib import ExitStack

import concourse.bass as bass
from concourse import mybir

F32 = mybir.dt.float32
F16 = mybir.dt.float16
BF16 = mybir.dt.bfloat16
I32 = mybir.dt.int32
ALU = mybir.AluOpType
ACT = mybir.ActivationFunctionType
AX = mybir.AxisListType.X
RMAX = bass.bass_isa.ReduceOp.max

P = 128
D = 128
N = 3125
NT = -(-N // P)
NP = NT * P
E = 100000
BLK = 512
CPB = BLK // P
NB = -(-E // BLK)
NC = NB * CPB
EP = NB * BLK
RP = NB // 2
NR = NT + 1
CEN = (NP + P) // 2
GT = 5
NG = NT // GT
GW = GT * P
HW = GW // 2
BANK = 512
MUL = 32
NBAS = 8
HID = 64
SEG = EP // (P // NBAS)
ZW = D + 2
SLOPE = 0.2
LN_EPS = 1e-5
TINY = 1e-30
A_BANKS = -(-NP // BANK)
SLICE = NP // CPB
LEAST = 3
TGROUPS = [(0, 7), (7, 13), (13, 19), (19, 25)]


def bank_cols(b):
    return b * BANK, min(NP, (b + 1) * BANK)


def gate(eng, sem, value, carrier):
    eng.wait_ge(sem, value)
    eng.sem_inc(carrier, 1)


class Memory:

    def __init__(self, nc, ctx, phase):
        self.nc, self.ctx, self.phase, self.numbers = nc, ctx, phase, []

    def sb(self, name, shape, dt=F32):
        return self.ctx.enter_context(self.nc.sbuf_tensor(f"{self.phase}_{name}", shape, dt))

    def ps(self, name, shape, dt=F32):
        return self.ctx.enter_context(self.nc.psum_tensor(f"{self.phase}_{name}", shape, dt))

    def sem(self, name):
        one = self.ctx.enter_context(self.nc.semaphore(f"{self.phase}_{name}"))
        self.numbers.append(one.num)
        return one

    def clear_at_exit(self):
        runs = []
        for num in sorted(self.numbers):
            if runs and runs[-1].stop == num:
                runs[-1] = range(runs[-1].start, num + 1)
            else:
                runs.append(range(num, num + 1))
        for run in runs:
            self.ctx.callback(self.nc.all_engine_barrier, sems_to_clear=run)

    def sems(self, names):
        return [self.sem(n) for n in names.split()]


class Steps:

    def __init__(self, eng, sem, carrier, base=0, per_turn=None):
        self.eng, self.sem, self.carrier, self.base, self.per_turn, self.n = eng, sem, carrier, base, per_turn, 0

    def done(self, ins):
        self.n += 1
        ins.then_inc(self.sem, 1)

    def wait(self):
        self.eng.wait_ge(self.sem, self.base + self.n)

    def wait_gated(self):
        gate(self.eng, self.sem, self.base + self.n, self.carrier)

    def close(self):
        assert self.n == self.per_turn, self.n


def load_range(eng, rng, t):
    lo = eng.value_load(rng[0:1, bass.ds(t, 1)], min_val=0, max_val=NB - LEAST)
    n = eng.value_load(rng[0:1, bass.ds(t + NR, 1)], min_val=LEAST, max_val=NB)
    cum = eng.value_load(rng[0:1, bass.ds(t + 2 * NR, 1)], min_val=0, max_val=NB * NR)
    return lo, n, cum


def prepare(nc, a, d, keep):
    with ExitStack() as ctx:
        mem = Memory(nc, ctx, "prep")
        sb, ps, sem = mem.sb, mem.ps, mem.sem
        dblk = sb("dblk", [RP, 2 * BLK], I32)
        bmin, bmax = sb("bmin", [RP, 2]), sb("bmax", [RP, 2])
        t_lo, t_hi = sb("t_lo", [RP, NR]), sb("t_hi", [RP, NR])
        b_up, b_down = sb("b_up", [RP, 2]), sb("b_down", [RP, 2])
        act1, act2 = sb("act1", [RP, NR, 2]), sb("act2", [RP, NR, 2])
        ext = sb("ext", [RP, 2 * NR])
        ext_all = sb("ext_all", [RP, 2 * NR])
        scan = [sb(f"scan{i}", [1, NR]) for i in range(2)]
        rng_f = sb("rng_f", [1, 3 * NR])
        w_oi = sb("w_oi", [P, D])
        wz = sb("wz", [P, ZW])
        a2 = sb("a2", [P, 2])
        vs_rep = sb("vs_rep", [P, P])
        xT = sb("xT", [P, NP])
        es_row, es_shift = sb("es_row", [P, NP]), sb("es_shift", [P, NP])
        part_f = sb("part_f", [P, 1])
        cols = sb("cols", [P, P])
        z = sb("z", [P, NT, ZW])
        rad = sb("rad", [P, SEG])
        rad_in = sb("rad_in", [P, SEG])
        basis = sb("basis", [P, SEG])
        part = sb("part", [P, 1], I32)
        part4 = sb("part4", [P, 1], I32)
        centre = sb("centre", [P, 1])
        vec = sb("vec", [P, NC, 3])
        sq = sb("sq", [P, NC, 3])
        nrm = sb("nrm", [P, NC])
        inv = sb("inv", [P, NC])
        unit = sb("unit", [P, NC, 3])
        ps_v = ps("ps_v", [P, BANK])
        ps_z = [ps(f"ps_z{i}", [P, BANK]) for i in range(2)]
        ps_e = [ps(f"ps_e{i}", [P, BANK]) for i in range(2)]
        carrier = sem("carrier")
        in_dst, in_w, in_x, in_len, in_vec = (sem(n) for n in ("in_dst", "in_w", "in_x", "in_len", "in_vec"))
        iotas, chain, extremes, reduced = (sem(n) for n in ("iotas", "chain", "extremes", "reduced"))
        v_ready, wz_ready, z_ready, z_copied, es_ready, es_copied = (
            sem(n) for n in ("v_ready", "wz_ready", "z_ready", "z_copied", "es_ready", "es_copied"))
        centre_ready, clipped, squared, exped, sumsq, rooted, basis_ready, unit_ready, z_all, stored = (
            sem(n) for n in ("centre_ready", "clipped", "squared", "exped", "sumsq", "rooted", "basis_ready",
                             "unit_ready", "z_all", "stored"))
        shifted = sem("shifted")
        ZB = 3
        groups = [(s, min(NT, s + ZB)) for s in range(0, NT, ZB)]
        mem.clear_at_exit()
        block = ctx.enter_context(nc.Block())

        @block.sync
        def _(sp):
            sp.dma_start(w_oi[:, :], a["w0"]).then_inc(in_w, 16)
            sp.dma_start(wz[:, 0:D], a["w0T"]).then_inc(in_w, 16)
            sp.dma_start(a2[:, 0:1], a["a_s"]).then_inc(in_w, 16)
            sp.dma_start(a2[:, 1:2], a["a_d"]).then_inc(in_w, 16)
            sp.dma_start(dblk[:, :], a["dst_blk"]).then_inc(in_dst, 16)
            sp.dma_start(xT[:, :], a["xT"]).then_inc(in_x, 16)
            for k in range(NBAS):
                q = P // NBAS
                sp.dma_start(rad_in[k * q:(k + 1) * q, :], a["radius"]).then_inc(in_len, 16)
            sp.dma_start(vec[:, :, :], a["vec"]).then_inc(in_vec, 16)
            sp.wait_ge(z_all, 1)
            sp.dma_start(d["z"], z[:, :, :]).then_inc(stored, 16)
            sp.wait_ge(shifted, 1)
            sp.dma_start(d["es_row"], es_shift[0:1, :]).then_inc(stored, 16)
            sp.wait_ge(basis_ready, 1)
            sp.dma_start(d["basis_pk"], basis[:, :]).then_inc(stored, 16)
            sp.wait_ge(unit_ready, 1)
            sp.dma_start(d["unit"], unit[:, :, :]).then_inc(stored, 16)
            sp.wait_ge(stored, 64)

        @block.gpsimd
        def _(pool):
            nc.gpsimd.iota(t_lo[:, :], pattern=[[P, NR]], base=0, channel_multiplier=0,
                           allow_small_or_imprecise_dtypes=True)
            nc.gpsimd.iota(t_hi[:, :], pattern=[[P, NR]], base=P, channel_multiplier=0,
                           allow_small_or_imprecise_dtypes=True)
            nc.gpsimd.iota(b_up[:, :], pattern=[[1, 2]], base=1, channel_multiplier=2,
                           allow_small_or_imprecise_dtypes=True)
            nc.gpsimd.iota(b_down[:, :], pattern=[[-1, 2]], base=NB, channel_multiplier=-2,
                           allow_small_or_imprecise_dtypes=True)
            nc.gpsimd.iota(cols[:, :], pattern=[[1, P]], base=0, channel_multiplier=0,
                           allow_small_or_imprecise_dtypes=True)
            nc.gpsimd.iota(part[:, :], pattern=[[0, 1]], base=0, channel_multiplier=1).then_inc(iotas, 1)
            pool.wait_ge(extremes, 1)
            nc.gpsimd.partition_all_reduce(ext_all[:, :], ext[:, :], RP, RMAX).then_inc(reduced, 1)

        @block.vector
        def _(dve):
            c = Steps(dve, chain, carrier)
            dve.wait_ge(in_dst, 16)
            dve.wait_ge(iotas, 1)
            c.done(nc.vector.tensor_copy(part_f[:, :], part[:, :]))
            c.done(nc.vector.tensor_scalar(part4[:, :], part[:, :], 4, None, ALU.arith_shift_right))
            c.wait()
            nc.vector.tensor_scalar(centre[:, :], part4[:, :], -1.0, None, ALU.mult).then_inc(centre_ready, 1)
            for ident in (keep["ident"], keep["ident_bf"]):
                c.done(nc.vector.tensor_scalar(ident[:, :], cols[:, :], part_f[:, 0:1], None, ALU.is_equal))
            dve.wait_ge(v_ready, 1)
            c.done(nc.vector.tensor_copy(wz[:, D:ZW], ps_v[:, 0:2]))
            c.wait()
            nc.vector.tensor_copy(vs_rep[:, :], wz[:, D:D + 1].to_broadcast([P, P])).then_inc(wz_ready, 1)
            dv = dblk[:, :].rearrange("p (b e) -> p b e", b=2)
            nc.vector.tensor_reduce(bmin[:, :], dv, AX, ALU.min)
            c.done(nc.vector.tensor_reduce(bmax[:, :], dv, AX, ALU.max))
            c.wait()

            def over_tiles(v):
                return v[:, :].rearrange("p (o b) -> p o b", o=1).to_broadcast([RP, NR, 2])

            def over_blocks(v):
                return v[:, :].rearrange("p (t o) -> p t o", o=1).to_broadcast([RP, NR, 2])

            nc.vector.tensor_tensor(act1[:, :, :], over_tiles(bmin), over_blocks(t_hi), ALU.is_lt)
            c.done(nc.vector.tensor_tensor(act2[:, :, :], over_tiles(bmax), over_blocks(t_lo), ALU.is_ge))
            c.wait()
            c.done(nc.vector.tensor_tensor(act1[:, :, :], act1[:, :, :], act2[:, :, :], ALU.mult))
            c.wait()
            c.done(nc.vector.tensor_tensor(act2[:, :, :], act1[:, :, :], over_tiles(b_down), ALU.mult))
            c.wait()
            c.done(nc.vector.tensor_reduce(ext[:, 0:NR], act2[:, :, :], AX, ALU.max))
            c.wait()
            c.done(nc.vector.tensor_tensor(act2[:, :, :], act1[:, :, :], over_tiles(b_up), ALU.mult))
            c.wait()
            nc.vector.tensor_reduce(ext[:, NR:2 * NR], act2[:, :, :], AX, ALU.max).then_inc(extremes, 1)
            for i, (s0, s1) in enumerate(groups):
                dve.wait_ge(z_ready, i + 1)
                ins = nc.vector.tensor_copy(z[:, s0:s1, :].rearrange("p t w -> p (t w)"),
                                            ps_z[i % 2][:, 0:(s1 - s0) * ZW])
                ins.then_inc(z_copied, 1)
            dve.wait_ge(z_copied, len(groups))
            dve.sem_inc(z_all, 1)
            dve.wait_ge(reduced, 1)
            lo, n, cum = (rng_f[:, i * NR:(i + 1) * NR] for i in range(3))
            c.done(nc.vector.tensor_scalar(lo, ext_all[0:1, 0:NR], -1.0, float(NB), ALU.mult, ALU.add))
            c.wait()
            c.done(nc.vector.tensor_scalar(lo, lo, float(NB - LEAST), None, ALU.min))
            c.wait()
            c.done(nc.vector.tensor_tensor(n, ext_all[0:1, NR:2 * NR], lo, ALU.subtract))
            c.wait()
            c.done(nc.vector.tensor_scalar(n, n, float(LEAST), None, ALU.max))
            c.wait()
            nc.vector.memset(scan[0][:, 0:1], 0.0)
            c.done(nc.vector.tensor_copy(scan[0][:, 1:NR], n[:, 0:NR - 1]))
            c.wait()
            step, k = 1, 0
            while step < NR:
                src, dst = scan[k % 2], scan[(k + 1) % 2]
                nc.vector.tensor_copy(dst[:, 0:step], src[:, 0:step])
                c.done(nc.vector.tensor_tensor(dst[:, step:NR], src[:, step:NR], src[:, 0:NR - step], ALU.add))
                c.wait()
                step, k = 2 * step, k + 1
            c.done(nc.vector.tensor_copy(cum, scan[k % 2][:, :]))
            c.wait()
            c.done(nc.vector.tensor_copy(keep["rng"][:, :], rng_f[:, :]))
            dve.wait_ge(es_copied, A_BANKS)
            c.done(nc.vector.tensor_reduce(keep["es_min"][:, :], es_row[:, :], AX, ALU.min))
            c.wait()
            nc.vector.tensor_scalar(es_shift[:, :], es_row[:, :], keep["es_min"][:, 0:1], None,
                                    ALU.subtract).then_inc(shifted, 1)
            dve.wait_ge(in_len, 16 * NBAS)
            nc.vector.tensor_scalar(rad[:, :], rad_in[:, :], 0.0, 1.0, ALU.max, ALU.min).then_inc(clipped, 1)
            dve.wait_ge(in_vec, 16)
            c.done(nc.vector.tensor_tensor(sq[:, :, :], vec[:, :, :], vec[:, :, :], ALU.mult))
            c.wait()
            nc.vector.tensor_reduce(nrm[:, :], sq[:, :, :], AX, ALU.add).then_inc(sumsq, 1)
            dve.wait_ge(rooted, 1)
            c.done(nc.vector.tensor_scalar(nrm[:, :], nrm[:, :], 1e-12, None, ALU.add))
            c.wait()
            c.done(nc.vector.reciprocal(inv[:, :], nrm[:, :]))
            c.wait()
            nc.vector.tensor_tensor(unit[:, :, :], vec[:, :, :],
                                    inv[:, :].rearrange("p (c o) -> p c o", o=1).to_broadcast([P, NC, 3]),
                                    ALU.mult).then_inc(unit_ready, 1)
            dve.wait_ge(exped, 1)
            nc.vector.scalar_tensor_tensor(basis[:, :], rad_in[:, :], 1.0, basis[:, :], ALU.is_le,
                                           ALU.mult).then_inc(basis_ready, 1)

        @block.scalar
        def _(act):
            for b in range(A_BANKS):
                c0, c1 = bank_cols(b)
                act.wait_ge(es_ready, b + 1)
                nc.scalar.copy(es_row[:, c0:c1], ps_e[b % 2][:, 0:c1 - c0]).then_inc(es_copied, 1)
            act.wait_ge(sumsq, 1)
            nc.scalar.activation(nrm[:, :], nrm[:, :], ACT.Sqrt).then_inc(rooted, 1)
            act.wait_ge(clipped, 1)
            act.wait_ge(centre_ready, 1)
            nc.scalar.activation(rad[:, :], rad[:, :], ACT.Square, bias=centre[:, 0:1],
                                 scale=float(NBAS - 1)).then_inc(squared, 1)
            act.wait_ge(squared, 1)
            nc.scalar.activation(basis[:, :], rad[:, :], ACT.Exp, scale=-0.5).then_inc(exped, 1)

        @block.tensor
        def _(pe):
            pe.wait_ge(in_w, 64)
            nc.tensor.matmul(ps_v[:, 0:2], w_oi[:, :], a2[:, :], start=True, stop=True).then_inc(v_ready, 1)
            pe.wait_ge(wz_ready, 1)
            pe.wait_ge(in_x, 16)
            for i, (s0, s1) in enumerate(groups):
                if i >= 2:
                    pe.wait_ge(z_copied, i - 1)
                for s in range(s0, s1):
                    last = nc.tensor.matmul(ps_z[i % 2][:, (s - s0) * ZW:(s - s0 + 1) * ZW],
                                            xT[:, s * P:(s + 1) * P], wz[:, :], start=True, stop=True)
                last.then_inc(z_ready, 1)
            for b in range(A_BANKS):
                c0, c1 = bank_cols(b)
                if b >= 2:
                    pe.wait_ge(es_copied, b - 1)
                nc.tensor.matmul(ps_e[b % 2][:, 0:c1 - c0], vs_rep[:, :], xT[:, c0:c1], start=True,
                                 stop=True).then_inc(es_ready, 1)


def build_counts(nc, a, d, keep, AT):
    with ExitStack() as ctx:
        mem = Memory(nc, ctx, "count")
        sb, ps, sem = mem.sb, mem.ps, mem.sem
        rng, es_max, deg = keep["rng"], keep["es_max"], keep["deg"]
        es_row = sb("es_row", [P, NP])
        iota = sb("iota", [P, NP + P], F16)
        src_c, dst_c = sb("src_c", [P, NC]), sb("dst_c", [P, NC])
        oh_src = [sb(f"oh_src{i}", [P, NP], BF16) for i in range(2)]
        oh_dst = [sb(f"oh_dst{i}", [P, P], BF16) for i in range(2)]
        A_sb = sb("A_sb", [P, NP], BF16)
        mask = sb("mask", [P, SLICE], BF16)
        slice_max = sb("slice_max", [P, CPB])
        bank_sum = sb("bank_sum", [P, NT * A_BANKS])
        ident = keep["ident_bf"]
        A_ps = ps("A_ps", [P, A_BANKS * BANK])
        T_ps = ps("T_ps", [P, 2 * BANK], BF16)
        raw = oh_src[0][:, 0:2 * NC].bitcast(I32)
        raw2 = oh_src[1][:, 0:2 * NC].bitcast(I32)
        carrier = sem("carrier")
        in_scores = sem("in_scores")
        in_edges, iotas, centred, oh_ready, oh_free = (
            sem(n) for n in ("in_edges", "iotas", "centred", "oh_ready", "oh_free"))
        a_copied, at_ready, at_copied, scored, chain = (
            sem(n) for n in ("a_copied", "at_ready", "at_copied", "scored", "chain"))
        mem.clear_at_exit()
        block = ctx.enter_context(nc.Block())
        RING = 2

        @block.sync
        def _(sp):
            sp.dma_start(es_row[:, :], d["es_row"].to_broadcast([P, NP])).then_inc(in_scores, 16)
            sp.dma_start(raw, a["src"]).then_inc(in_edges, 16)
            sp.dma_start(raw2, a["dst"]).then_inc(in_edges, 16)

        @block.gpsimd
        def _(pool):
            nc.gpsimd.iota(iota[:, :], pattern=[[1, NP + P]], base=-CEN, channel_multiplier=0,
                           allow_small_or_imprecise_dtypes=True).then_inc(iotas, 1)

        def one_hot(dve, b, q, k, t):
            c = nc.s_assert_within(b * CPB + k, 0, NC - 1)
            dve.wait_ge(oh_free, q * CPB + k + 1)
            nc.vector.tensor_scalar(oh_src[k % RING][:, :], iota[:, 0:NP], src_c[:, bass.ds(c, 1)], None,
                                    ALU.is_equal)
            nc.vector.tensor_scalar(oh_dst[k % RING][:, :], iota[:, bass.ds(t * P, P)],
                                    dst_c[:, bass.ds(c, 1)], None, ALU.is_equal).then_inc(oh_ready, 1)

        @block.vector
        def _(dve):
            dve.wait_ge(in_edges, 32)
            nc.vector.tensor_scalar(src_c[:, :], raw, float(-CEN), None, ALU.add)
            nc.vector.tensor_scalar(dst_c[:, :], raw2, float(-CEN), None, ALU.add).then_inc(centred, 1)
            dve.wait_ge(centred, 1)
            dve.wait_ge(iotas, 1)
            dve.wait_ge(in_scores, 16)
            dve.sem_inc(oh_free, RING)
            lo, n, cum = load_range(dve, rng, 0)
            for j in range(2):
                for k in range(CPB):
                    one_hot(dve, lo + j, cum + j, k, 0)
            with dve.Fori(0, NT) as t:
                lo, n, cum = load_range(dve, rng, t)
                with dve.Fori(2, n) as j:
                    for k in range(CPB):
                        one_hot(dve, lo + j, cum + j, k, t)
                lo, n, cum = load_range(dve, rng, t + 1)
                for k in range(CPB):
                    one_hot(dve, lo, cum, k, t + 1)
                gate(dve, a_copied, A_BANKS * (t + 1), carrier)
                c = Steps(dve, chain, carrier, base=t * (2 * CPB + 1), per_turn=2 * CPB + 1)
                for k in range(CPB):
                    one_hot(dve, lo + 1, cum + 1, k, t + 1)
                    cols = slice(k * SLICE, (k + 1) * SLICE)
                    c.done(nc.vector.tensor_scalar(mask[:, :], A_sb[:, cols], 1.0, None, ALU.min))
                    c.wait_gated()
                    c.done(nc.vector.tensor_tensor_reduce(out=mask[:, :], in0=mask[:, :], in1=es_row[:, cols],
                                                          scale=1.0, scalar=0.0, op0=ALU.mult, op1=ALU.max,
                                                          accum_out=slice_max[:, k:k + 1]))
                    c.wait_gated()
                c.done(nc.vector.tensor_reduce(es_max[:, bass.ds(t, 1)], slice_max[:, :], AX, ALU.max))
                c.wait_gated()
                c.close()
                dve.sem_inc(scored, 1)
            dve.wait_ge(a_copied, NT * A_BANKS)
            nc.vector.tensor_reduce(deg[:, :], bank_sum[:, :].rearrange("p (t b) -> p t b", b=A_BANKS), AX, ALU.add)

        @block.scalar
        def _(act):
            act.sem_inc(at_copied, 1)
            act.sem_inc(scored, 1)
            with act.Fori(0, NT) as t:
                lo, n, cum = load_range(act, rng, t)
                gate(act, oh_free, (cum + n) * CPB + RING, carrier)
                for b in range(A_BANKS):
                    if b == 0:
                        gate(act, scored, t + 1, carrier)
                    c0, c1 = bank_cols(b)
                    nc.scalar.activation(A_sb[:, c0:c1], A_ps[:, c0:c1], ACT.Copy,
                                         accum_out=bank_sum[:, bass.ds(t * A_BANKS + b, 1)]).then_inc(a_copied, 1)
                for g, (s0, s1) in enumerate(TGROUPS):
                    act.wait_ge(at_ready, t * len(TGROUPS) + g + 1)
                    nc.scalar.copy(AT[:, s0:s1, bass.ds(t * P, P)],
                                   T_ps[:, 0:(s1 - s0) * P].rearrange("p (s d) -> p s d", d=P)
                                   ).then_inc(at_copied, 1)

        @block.tensor
        def _(pe):
            def chunk(q, k, first=False, t_done=None):
                pe.wait_ge(oh_ready, q * CPB + k + 1)
                for b in range(A_BANKS):
                    c0, c1 = bank_cols(b)
                    if first and t_done is not None:
                        pe.wait_ge(a_copied, t_done * A_BANKS + b + 1)
                    last = nc.tensor.matmul(A_ps[:, c0:c1], oh_dst[k % RING][:, :], oh_src[k % RING][:, c0:c1],
                                            start=first, stop=True, skip_group_check=True)
                last.then_inc(oh_free, 1)

            for j in range(2):
                for k in range(CPB):
                    chunk(j, k, first=(j == 0 and k == 0))
            with pe.Fori(0, NT) as t:
                lo, n, cum = load_range(pe, rng, t)
                with pe.Fori(2, n) as j:
                    for k in range(CPB):
                        chunk(cum + j, k)
                for k in range(CPB):
                    chunk(cum + n, k, first=(k == 0), t_done=t)
                    for g in ([k - 1] if k < CPB - 1 else [k - 1, k]):
                        if g < 0:
                            continue
                        s0, s1 = TGROUPS[g]
                        pe.wait_ge(at_copied, t * len(TGROUPS) + g + 1)
                        for s in range(s0, s1):
                            last = nc.tensor.transpose(T_ps[:, (s - s0) * P:(s - s0 + 1) * P],
                                                       A_sb[:, s * P:(s + 1) * P], ident[:, :])
                        last.then_inc(at_ready, 1)
                for k in range(CPB):
                    chunk(cum + n + 1, k)


class NormBuffers:

    def __init__(self, mem, tag, eps):
        self.stats = mem.sb(f"{tag}_stats", [P, GT, 6])
        self.mv = mem.sb(f"{tag}_mv", [P, GT, 2])
        self.var = mem.sb(f"{tag}_var", [P, GT])
        self.std = mem.sb(f"{tag}_std", [P, GT])
        self.rstd = mem.sb(f"{tag}_rstd", [P, GT])
        self.var_ready, self.std_ready = mem.sem(f"{tag}_var_ready"), mem.sem(f"{tag}_std_ready")
        self.eps = eps


NORM_STEPS = 4


def norm_on_vector(nc, dve, c, nb, turn, src, dst):
    for r in range(GT):
        last = nc.vector.bn_stats(nb.stats[:, r, :], src[:, r, :])
    c.done(last)
    c.wait_gated()
    for r in range(GT):
        last = nc.vector.bn_aggr(nb.mv[:, r, :], nb.stats[:, r, :])
    c.done(last)
    c.wait()
    nc.vector.tensor_scalar(nb.var[:, :], nb.mv[:, :, 1], nb.eps, None, ALU.add).then_inc(nb.var_ready, 1)
    dve.wait_ge(nb.std_ready, turn + 1)
    c.done(nc.vector.reciprocal(nb.rstd[:, :], nb.std[:, :]))
    c.wait()
    for r in range(GT):
        last = nc.vector.tensor_scalar(dst[:, r, :], src[:, r, :], nb.mv[:, r, 0:1], nb.rstd[:, r:r + 1],
                                       ALU.subtract, ALU.mult)
    c.done(last)


def norm_on_scalar(nc, act, nb, turn):
    act.wait_ge(nb.var_ready, turn + 1)
    nc.scalar.activation(nb.std[:, :], nb.var[:, :], ACT.Sqrt).then_inc(nb.std_ready, 1)


def attention(nc, a, d, keep, AT):
    with ExitStack() as ctx:
        mem = Memory(nc, ctx, "att")
        sb, ps, sem = mem.sb, mem.ps, mem.sem
        z = sb("z", [P, NT, ZW])
        es, es_low, ed, u, ul = (sb(n, [P, NT]) for n in ("es", "es_low", "ed", "u", "ul"))
        row_c = sb("row_c", [P, 2, NT])
        rows_t = sb("rows_t", [NT, 2 * P])
        rows = sb("rows", [P, 2, GW])
        e1 = [sb(f"e1_{k}", [P, GW]) for k in range(GT)]
        E2R = 3
        e2 = [sb(f"e2_{k}", [P, GW]) for k in range(E2R)]
        xg, x1g, x1T = sb("xg", [P, GT, D]), sb("x1g", [P, GT, D]), sb("x1T", [P, GT, P])
        up = sb("up", [P, D])
        den, rec = sb("den", [P, GT]), sb("rec", [P, GT])
        nb = NormBuffers(mem, "ln", LN_EPS)
        acc = ps("acc", [P, GT * BANK])
        px = ps("px", [P, 3 * BANK])
        acc_v = acc[:, :].rearrange("p (r c) -> p r c", c=BANK)
        carrier, chain, chain0 = mem.sems("carrier chain chain0")
        in_z, in_up, rows_c, rows_tp, rows_copied, rows_stored, in_rows, in_x = mem.sems(
            "in_z in_up rows_c rows_tp rows_copied rows_stored in_rows in_x")
        e_ready, q_done, p_ready, p_used, z_ready, up_ready, up_zero = mem.sems(
            "e_ready q_done p_ready p_used z_ready up_ready up_zero")
        acc_done, acc_free, x1_ready, x1t_ready, x1t_copied, tab_ready, tab_copied, stored = mem.sems(
            "acc_done acc_free x1_ready x1t_ready x1t_copied tab_ready tab_copied stored")
        table = d["table"].rearrange("(t p) f -> p t f", p=P)
        x_v = a["x"].rearrange("(t p) f -> p t f", p=P)
        x1_v = d["x1"].rearrange("(t p) f -> p t f", p=P)
        mem.clear_at_exit()
        block = ctx.enter_context(nc.Block())

        def rows_of(g):
            src = d["rows"][:, bass.ds(g * GW, GW)].rearrange("(o r) w -> o r w", o=1)
            return src.to_broadcast([P, 2, GW])

        @block.sync
        def _(sp):
            sp.dma_start(z[:, :, :], d["z"]).then_inc(in_z, 16)
            sp.wait_ge(up_zero, 1)
            sp.dma_start(up[0:MUL, 0:MUL], a["up0"]).then_inc(in_up, 16)
            for c in range(3):
                sp.dma_start(up[MUL + c:P:3, MUL * (c + 1):MUL * (c + 2)], a["up1"]).then_inc(in_up, 16)
            sp.wait_ge(rows_copied, 1)
            sp.dma_start(d["rows"][0:1, :].rearrange("o (t p) -> (o t) p", p=P),
                         rows_t[:, 0:P]).then_inc(rows_stored, 16)
            sp.dma_start(d["rows"][1:2, :].rearrange("o (t p) -> (o t) p", p=P),
                         rows_t[:, P:2 * P]).then_inc(rows_stored, 16)
            sp.wait_ge(rows_stored, 32)
            sp.dma_start(rows[:, :, :], rows_of(0)).then_inc(in_rows, 16)
            with sp.Fori(1, NG) as g:
                sp.wait_ge(e_ready, g * NT)
                sp.dma_start(rows[:, :, :], rows_of(g)).then_inc(in_rows, 16)

        @block.gpsimd
        def _(pool):
            with pool.Fori(0, NG) as g:
                nc.gpsimd.dma_start(xg[:, :, :], x_v[:, bass.ds(g * GT, GT), :]).then_inc(in_x, 16)
                gate(pool, x1_ready, g + 1, carrier)
                nc.gpsimd.dma_start(x1_v[:, bass.ds(g * GT, GT), :], x1g[:, :, :]).then_inc(stored, 16)
                gate(pool, tab_copied, g + 1, carrier)
                nc.gpsimd.dma_start(table[:, bass.ds(g * GT, GT), :], xg[:, :, :]).then_inc(stored, 16)
                gate(pool, stored, 32 * (g + 1), carrier)

        @block.scalar
        def _(act):
            act.wait_ge(z_ready, 1)
            with act.Fori(0, NG) as g:
                gate(act, in_rows, 16 * (g + 1), carrier)
                with act.Fori(0, GT) as i:
                    for k in range(GT):
                        s = i * GT + k
                        w = g * NT + s
                        gate(act, p_used, w + 1, carrier)
                        nc.scalar.activation(e1[k][:, :], rows[:, 0, :], ACT.Exp, bias=es[:, bass.ds(s, 1)])
                        gate(act, q_done, w + 1, carrier)
                        nc.scalar.activation(e2[k % E2R][:, :], rows[:, 1, :], ACT.Exp,
                                             bias=es_low[:, bass.ds(s, 1)]).then_inc(e_ready, 1)
                norm_on_scalar(nc, act, nb, g)

        @block.vector
        def _(dve):
            c = Steps(dve, chain0, carrier)
            nc.vector.memset(up[:, :], 0.0).then_inc(up_zero, 1)
            dve.wait_ge(in_z, 16)
            nc.vector.tensor_copy(es[:, :], z[:, :, D])
            nc.vector.tensor_scalar(es_low[:, :], z[:, :, D], SLOPE, None, ALU.mult)
            nc.vector.tensor_copy(ed[:, :], z[:, :, D + 1])
            c.done(nc.vector.tensor_scalar(u[:, :], keep["es_max"][:, :], keep["es_min"][:, 0:1], None, ALU.add))
            c.wait()
            nc.vector.memset(z[:, :, D:D + 1], 1.0)
            c.done(nc.vector.tensor_tensor(u[:, :], u[:, :], ed[:, :], ALU.add))
            c.wait()
            c.done(nc.vector.tensor_scalar(ul[:, :], u[:, :], SLOPE, None, ALU.mult))
            c.wait()
            c.done(nc.vector.tensor_tensor(u[:, :], u[:, :], ul[:, :], ALU.max))
            c.wait()
            nc.vector.tensor_tensor(row_c[:, 0, :], ed[:, :], u[:, :], ALU.subtract)
            nc.vector.scalar_tensor_tensor(row_c[:, 1, :], ed[:, :], SLOPE, u[:, :], ALU.mult,
                                           ALU.subtract).then_inc(rows_c, 1)
            dve.sem_inc(z_ready, 1)
            dve.wait_ge(rows_tp, 1)
            nc.vector.tensor_copy(rows_t[:, :], px[0:NT, 0:2 * P]).then_inc(rows_copied, 1)
            dve.wait_ge(in_up, 64)
            nc.vector.tensor_scalar(up[:, :], up[:, :], MUL ** -0.5, None, ALU.mult).then_inc(up_ready, 1)
            dve.sem_inc(p_used, GT)
            dve.sem_inc(q_done, 2)
            dve.sem_inc(acc_free, 1)
            per_turn = 3 + NORM_STEPS
            with dve.Fori(0, NG) as g:
                with dve.Fori(0, GT) as i:
                    for k in range(GT):
                        s = i * GT + k
                        w = g * NT + s
                        dve.wait_ge(e_ready, w + 1)
                        nc.vector.scalar_tensor_tensor(e1[k][:, :], e1[k][:, :], 1.0, e2[k % E2R][:, :], ALU.min,
                                                       ALU.max).then_inc(q_done, 1)
                        dve.wait_ge(q_done, w + 3)
                        nc.vector.scalar_tensor_tensor(e1[k][:, :], e1[k][:, :], 1.0,
                                                       AT[:, bass.ds(s, 1), bass.ds(g * GW, GW)]
                                                       .rearrange("p o w -> p (o w)"),
                                                       ALU.min, ALU.mult).then_inc(p_ready, 1)
                c = Steps(dve, chain, carrier, base=g * per_turn, per_turn=per_turn)
                dve.wait_ge(acc_done, g + 1)
                c.done(nc.vector.tensor_scalar(den[:, :], acc_v[:, :, D], TINY, None, ALU.max))
                c.wait()
                c.done(nc.vector.reciprocal(rec[:, :], den[:, :]))
                c.wait()
                gate(dve, in_x, 16 * (g + 1), carrier)
                for r in range(GT):
                    last = nc.vector.scalar_tensor_tensor(xg[:, r, :], acc_v[:, r, 0:D], rec[:, r:r + 1],
                                                          xg[:, r, :], ALU.mult, ALU.add)
                c.done(last)
                c.wait_gated()
                dve.sem_inc(acc_free, 1)
                norm_on_vector(nc, dve, c, nb, g, xg, x1g)
                c.wait_gated()
                dve.sem_inc(x1_ready, 1)
                c.close()
                dve.wait_ge(x1t_ready, g + 1)
                nc.vector.tensor_copy(x1T[:, :, :].rearrange("p t f -> p (t f)"), px[:, 0:GW]).then_inc(x1t_copied, 1)
                dve.wait_ge(tab_ready, g + 1)
                nc.vector.tensor_copy(xg[:, :, :].rearrange("p t f -> p (t f)"), px[:, GW:2 * GW]
                                      ).then_inc(tab_copied, 1)

        @block.tensor
        def _(pe):
            pe.wait_ge(rows_c, 1)
            for i in range(2):
                last = nc.tensor.transpose(px[0:NT, i * P:(i + 1) * P], row_c[:, i, :], keep["ident"][:, :])
            last.then_inc(rows_tp, 1)
            pe.wait_ge(up_ready, 1)

            def five(g, i, first):
                for k in range(GT):
                    s = i * GT + k
                    pe.wait_ge(p_ready, g * NT + s + 1)
                    for r in range(GT):
                        last = nc.tensor.matmul(acc_v[:, r, 0:D + 1], e1[k][:, r * P:(r + 1) * P],
                                                z[:, bass.ds(s, 1), 0:D + 1].rearrange("p o w -> p (o w)"),
                                                start=first and k == 0, stop=True, skip_group_check=True)
                    last.then_inc(p_used, 1)

            with pe.Fori(0, NG) as g:
                gate(pe, acc_free, g + 1, carrier)
                five(g, 0, True)
                with pe.Fori(1, GT) as i:
                    five(g, i, False)
                gate(pe, p_used, GT + (g + 1) * NT, carrier)
                pe.sem_inc(acc_done, 1)
                gate(pe, x1_ready, g + 1, carrier)
                for r in range(GT):
                    last = nc.tensor.transpose(px[:, r * P:(r + 1) * P], x1g[:, r, :], keep["ident"][:, :])
                last.then_inc(x1t_ready, 1)
                gate(pe, x1t_copied, g + 1, carrier)
                for r in range(GT):
                    last = nc.tensor.matmul(px[:, GW + r * P:GW + (r + 1) * P], x1T[:, r, :], up[:, :],
                                            start=True, stop=True, skip_group_check=True)
                last.then_inc(tab_ready, 1)


def edge_messages(nc, a, d, keep):
    with ExitStack() as ctx:
        mem = Memory(nc, ctx, "edge")
        sb, ps, sem = mem.sb, mem.ps, mem.sem
        rng = keep["rng"]
        U = 2
        CPU = CPB // U
        iota = sb("iota", [P, NP], F16)
        src_i, dst_i, dst_c = sb("src_i", [P, NC], I32), sb("dst_i", [P, NC], I32), sb("dst_c", [P, NC])
        unit = sb("unit", [P, NC, 3])
        basis = sb("basis", [NBAS, BLK])
        w0, b0, w1, b1 = sb("w0", [NBAS, HID]), sb("b0", [HID, 1]), sb("w1", [HID, HID]), sb("b1", [HID, 1])
        w2 = sb("w2", [HID + 1, D])
        h1, h2 = sb("h1", [HID, BLK]), sb("h2", [HID + 1, BLK])
        idx = [sb(f"idx{u}", [P, CPU], I32) for u in range(U)]
        G = [sb(f"G{u}", [P, CPU, D]) for u in range(U)]
        oh = [sb(f"oh{u}", [P, CPU, P]) for u in range(U)]
        midA = [sb(f"midA{u}", [P, CPU, D]) for u in range(U)]
        midB = [sb(f"midB{u}", [P, CPU, D]) for u in range(U)]
        sw, along, dot = sb("sw", [P, CPU, MUL]), sb("along", [P, CPU, 3, MUL]), sb("dot", [P, CPU, MUL])
        msg = sb("msg", [P, 2, P])
        h1p, h2p = ps("h1p", [P, BANK]), ps("h2p", [P, BANK])
        wp = [ps(f"wp{u}", [P, BANK]) for u in range(U)]
        accA, accB = ps("accA", [P, BANK]), ps("accB", [P, BANK])
        carrier, chain, idx_copied, iotas, in_edges, in_w, in_unit, centred, scaled = mem.sems(
            "carrier chain idx_copied iotas in_edges in_w in_unit centred scaled")
        basis_in, h1p_ready, h1_ready, h2p_ready, h2_ready, w_ready = mem.sems(
            "basis_in h1p_ready h1_ready h2p_ready h2_ready w_ready")
        g_used, mid_ready, mid_used, acc_free, msg_copied, stored = mem.sems(
            "g_used mid_ready mid_used acc_free msg_copied stored")
        gathered = [[sem(f"gathered{u}{k}") for k in range(CPU)] for u in range(U)]
        mem.clear_at_exit()
        block = ctx.enter_context(nc.Block())

        @block.sync
        def _(sp):
            sp.dma_start(src_i[:, :], a["src"]).then_inc(in_edges, 16)
            sp.dma_start(dst_i[:, :], a["dst"]).then_inc(in_edges, 16)
            for dst, src in ((w0, "mw0"), (b0, "mb0"), (w1, "mw1"), (b1, "mb1")):
                sp.dma_start(dst[:, :], a[src]).then_inc(in_w, 16)
            sp.dma_start(w2[0:HID, :], a["mw2"]).then_inc(in_w, 16)
            sp.dma_start(w2[HID:HID + 1, :], a["mb2"]).then_inc(in_w, 16)
            sp.dma_start(unit[:, :, :], d["unit"]).then_inc(in_unit, 16)

            def load(b, q):
                sp.dma_start(basis[:, :], d["basis"][:, bass.ds(b * BLK, BLK)]).then_inc(basis_in, 16)
                gate(sp, h1p_ready, q + 1, carrier)

            with sp.Fori(0, NT) as t:
                lo, n, cum = load_range(sp, rng, t)
                with sp.Fori(0, n) as j:
                    load(nc.s_assert_within(lo + j, 0, NB - 1), cum + j)
            lo, n, cum = load_range(sp, rng, NT)
            for j in range(2):
                load(lo + j, cum + j)

        @block.gpsimd
        def _(pool):
            nc.gpsimd.iota(iota[:, :], pattern=[[1, NP]], base=-CEN, channel_multiplier=0,
                           allow_small_or_imprecise_dtypes=True).then_inc(iotas, 1)
            pool.wait_ge(in_edges, 32)
            with pool.Fori(0, NT) as t:
                lo, n, cum = load_range(pool, rng, t)
                with pool.Fori(0, n) as j:
                    q = cum + j
                    for u in range(U):
                        c = nc.s_assert_within((lo + j) * CPB + u * CPU, 0, NC - CPU)
                        gate(pool, g_used, q * U + u + 1, carrier)
                        nc.gpsimd.tensor_copy(idx[u][:, :], src_i[:, bass.ds(c, CPU)]).then_inc(idx_copied, 1)
                        gate(pool, idx_copied, q * U + u + 1, carrier)
                        for k in range(CPU):
                            nc.gpsimd.indirect_dma_start(
                                out=G[u][:, k, :], out_offset=None, in_=d["table"],
                                in_offset=bass.IndirectOffsetOnAxis(ap=idx[u][:, k:k + 1], axis=0),
                            ).then_inc(gathered[u][k], 16)

        @block.scalar
        def _(act):
            act.wait_ge(in_w, 96)

            def silus(q):
                act.wait_ge(h1p_ready, q + 1)
                nc.scalar.activation(h1[:, :], h1p[0:HID, :], ACT.Silu, bias=b0[:, 0:1]).then_inc(h1_ready, 1)
                act.wait_ge(h2p_ready, q + 1)
                nc.scalar.activation(h2[0:HID, :], h2p[0:HID, :], ACT.Silu, bias=b1[:, 0:1]).then_inc(h2_ready, 1)

            silus(0)
            silus(1)
            with act.Fori(0, NT) as t:
                lo, n, cum = load_range(act, rng, t)
                with act.Fori(0, n) as j:
                    silus(cum + j + 2)
                gate(act, mid_used, (cum + n) * U + U, carrier)
                nc.scalar.copy(msg[:, 0, :], accA[:, 0:P])
                nc.scalar.copy(msg[:, 1, :], accB[:, 0:P]).then_inc(msg_copied, 1)
                gate(act, msg_copied, t + 1, carrier)
                act.sem_inc(acc_free, 1)
                act.dma_start(d["msg"][:, bass.ds(t, 1), :, :].rearrange("p o h w -> p (o h) w"),
                              msg[:, :, :]).then_inc(stored, 16)
                act.wait_ge(stored, 16 * (t + 1))
                act.sem_inc(carrier, 1)

        @block.vector
        def _(dve):
            dve.wait_ge(in_w, 96)
            nc.vector.tensor_scalar(w0[:, :], w0[:, :], float(NBAS) ** 0.5, None, ALU.mult)
            nc.vector.memset(h2[HID:HID + 1, :], 1.0).then_inc(scaled, 1)
            dve.wait_ge(in_edges, 32)
            nc.vector.tensor_scalar(dst_c[:, :], dst_i[:, :], float(-CEN), None, ALU.add).then_inc(centred, 1)
            dve.wait_ge(centred, 1)
            dve.wait_ge(iotas, 1)
            dve.wait_ge(in_unit, 16)
            dve.sem_inc(g_used, U)
            dve.sem_inc(mid_used, U)
            per_turn = 4

            def spread(x, i, c, w):
                return (x.rearrange("p k (o w) -> p k o w", o=1) if i == 0 else
                        x.rearrange("p k (c o) -> p k c o", o=1)).to_broadcast([P, CPU, c, w])

            with dve.Fori(0, NT) as t:
                lo, n, cum = load_range(dve, rng, t)
                with dve.Fori(0, n) as j:
                    q = cum + j
                    for u in range(U):
                        v = q * U + u
                        c0 = nc.s_assert_within((lo + j) * CPB + u * CPU, 0, NC - CPU)
                        st = Steps(dve, chain, carrier, base=v * per_turn, per_turn=per_turn)
                        dve.wait_ge(mid_used, v + 1)
                        for k in range(CPU):
                            nc.vector.tensor_scalar(oh[u][:, k, :], iota[:, bass.ds(t * P, P)],
                                                    dst_c[:, bass.ds(c0 + k, 1)], None, ALU.is_equal)
                        for k in range(CPU):
                            gate(dve, gathered[u][k], 16 * (q + 1), carrier)
                        s, vec = G[u][:, :, 0:MUL], G[u][:, :, MUL:D].rearrange("p k (c w) -> p k c w", c=3)
                        un = spread(unit[:, bass.ds(c0, CPU), :], 1, 3, MUL)
                        w = [wp[u][:, 0:CPU * D].rearrange("p (k w) -> p k w", w=D)[:, :, i * MUL:(i + 1) * MUL]
                             for i in range(4)]
                        A, B = midA[u], midB[u]
                        outA = A[:, :, MUL:D].rearrange("p k (c w) -> p k c w", c=3)
                        outB = B[:, :, MUL:D].rearrange("p k (c w) -> p k c w", c=3)
                        st.done(nc.vector.tensor_tensor(along[:, :, :, :], vec, un, ALU.mult))
                        dve.wait_ge(w_ready, v + 1)
                        st.done(nc.vector.tensor_tensor(sw[:, :, :], s, w[1], ALU.mult))
                        nc.vector.tensor_tensor(A[:, :, 0:MUL], s, w[0], ALU.mult)
                        st.wait()
                        st.done(nc.vector.tensor_reduce(dot[:, :, :], along[:, :, :, :].rearrange("p k c w -> p k w c"),
                                                        AX, ALU.add))
                        nc.vector.tensor_tensor(outA, spread(sw[:, :, :], 0, 3, MUL), un, ALU.mult)
                        st.done(nc.vector.tensor_tensor(outB, vec, spread(w[2], 0, 3, MUL), ALU.mult))
                        st.wait()
                        nc.vector.tensor_tensor(B[:, :, 0:MUL], dot[:, :, :], w[3], ALU.mult).then_inc(mid_ready, 1)
                        st.close()
                        gate(dve, mid_ready, v + 1, carrier)
                        dve.sem_inc(g_used, 1)

        @block.tensor
        def _(pe):
            pe.wait_ge(scaled, 1)
            pe.wait_ge(in_w, 96)

            def mlp1(q):
                pe.wait_ge(basis_in, 16 * (q + 1))
                nc.tensor.matmul(h1p[0:HID, :], w0[:, :], basis[:, :], start=True, stop=True).then_inc(h1p_ready, 1)

            def mlp2(q):
                gate(pe, h1_ready, q + 1, carrier)
                nc.tensor.matmul(h2p[0:HID, :], w1[:, :], h1[:, :], start=True, stop=True).then_inc(h2p_ready, 1)

            def mlp3(q, u):
                pe.wait_ge(h2_ready, q + 1)
                for k in range(CPU):
                    c = u * CPU + k
                    last = nc.tensor.matmul(wp[u][:, k * D:(k + 1) * D], h2[:, c * P:(c + 1) * P], w2[:, :],
                                            start=True, stop=True, skip_group_check=True)
                last.then_inc(w_ready, 1)

            def scatter(q, u, first):
                pe.wait_ge(mid_ready, q * U + u + 1)
                for k in range(CPU):
                    for acc, mid in ((accA, midA), (accB, midB)):
                        last = nc.tensor.matmul(acc[:, 0:P], mid[u][:, k, :], oh[u][:, k, :],
                                                start=first and k == 0, stop=True, skip_group_check=True)
                last.then_inc(mid_used, 1)

            def step(q, first):
                scatter(q, 0, first)
                mlp3(q + 1, 0)
                mlp1(q + 2)
                scatter(q, 1, False)
                mlp3(q + 1, 1)
                mlp2(q + 2)

            mlp1(0)
            mlp2(0)
            mlp3(0, 0)
            mlp3(0, 1)
            mlp1(1)
            mlp2(1)
            pe.sem_inc(acc_free, 1)
            with pe.Fori(0, NT) as t:
                lo, n, cum = load_range(pe, rng, t)
                gate(pe, acc_free, t + 1, carrier)
                step(cum, True)
                with pe.Fori(1, n) as j:
                    step(cum + j, False)


def tiles_view(t):
    return t.rearrange("(t p) f -> p t f", p=P)


def flat(x):
    return x.rearrange("p t f -> p (t f)")


SPLIT_STEPS = 4


def split_on_vector(nc, c, src, rest, tabs, g):
    hi, mid, lo = (t[:, bass.ds(g * GT, GT), :] for t in tabs)
    c.done(nc.vector.tensor_copy(hi, src[:, :, :]))
    c.wait()
    c.done(nc.vector.tensor_tensor(rest[:, :, :], src[:, :, :], hi, ALU.subtract))
    c.wait()
    c.done(nc.vector.tensor_copy(mid, rest[:, :, :]))
    c.wait()
    c.done(nc.vector.tensor_tensor(lo, rest[:, :, :], mid, ALU.subtract))


def aggregate(nc, agg, tabs, AT, g):
    for s in range(NT):
        for i, tab in enumerate(tabs):
            for h in range(2):
                last = nc.tensor.matmul(agg[:, h * BANK:h * BANK + HW], tab[:, s, :],
                                        AT[:, s, bass.ds(g * GW + h * HW, HW)],
                                        start=(s == 0 and i == 0), stop=(s == NT - 1 and i == len(tabs) - 1))
    return last


def halves(agg):
    return agg[:, :].rearrange("p (h c) -> p h c", c=BANK)[:, :, 0:HW]


def update_messages(nc, a, d, keep, tabs):
    with ExitStack() as ctx:
        mem = Memory(nc, ctx, "upd")
        sb, ps = mem.sb, mem.ps
        raw, wo = sb("raw", [P, 2, MUL]), sb("wo", [P, 2, D])
        msg = sb("msg", [P, GT, 2 * P])
        xg, x2g, rest = sb("xg", [P, GT, D]), sb("x2g", [P, GT, D]), sb("rest", [P, GT, D])
        root, has = sb("root", [P, NT]), sb("has", [P, NT])
        dis_t = sb("dis_t", [NT, P])
        nb = NormBuffers(mem, "ln", LN_EPS)
        px = ps("px", [P, 2 * BANK])
        pt = ps("pt", [P, BANK])
        carrier, chain, chain0, in_w, in_msg, in_x, out_ready, x2_ready, stored, wo_ready = mem.sems(
            "carrier chain chain0 in_w in_msg in_x out_ready x2_ready stored wo_ready")
        deg_cut, rooted, dis_ready, dis_tp, dis_copied, dis_stored = mem.sems(
            "deg_cut rooted dis_ready dis_tp dis_copied dis_stored")
        x1_v, x2_v = tiles_view(d["x1"]), tiles_view(d["x2"])
        mem.clear_at_exit()
        block = ctx.enter_context(nc.Block())

        @block.sync
        def _(sp):
            for h in range(2):
                rows = slice(h * MUL, (h + 1) * MUL)
                sp.dma_start(raw[0:MUL, h, :], a["out0"][rows, :]).then_inc(in_w, 16)
                for c in range(3):
                    sp.dma_start(raw[MUL * (c + 1):MUL * (c + 2), h, :], a["out1"][rows, :]).then_inc(in_w, 16)
            sp.wait_ge(dis_copied, 1)
            sp.dma_start(d["dis"].rearrange("o (t p) -> (o t) p", p=P), dis_t[:, :]).then_inc(dis_stored, 16)
            with sp.Fori(0, NG) as g:
                sp.dma_start(msg[:, :, :], d["msg"][:, bass.ds(g * GT, GT), :, :]
                             .rearrange("p t h w -> p t (h w)")).then_inc(in_msg, 16)
                sp.dma_start(xg[:, :, :], x1_v[:, bass.ds(g * GT, GT), :]).then_inc(in_x, 16)
                sp.wait_ge(x2_ready, g + 1)
                sp.dma_start(x2_v[:, bass.ds(g * GT, GT), :], x2g[:, :, :]).then_inc(stored, 16)
                gate(sp, stored, 16 * (g + 1), carrier)
            sp.wait_ge(dis_stored, 16)

        @block.scalar
        def _(act):
            act.wait_ge(deg_cut, 1)
            nc.scalar.activation(root[:, :], root[:, :], ACT.Sqrt).then_inc(rooted, 1)
            with act.Fori(0, NG) as g:
                norm_on_scalar(nc, act, nb, g)

        @block.vector
        def _(dve):
            c = Steps(dve, chain0, carrier)
            c.done(nc.vector.tensor_scalar(root[:, :], keep["deg"][:, :], 1.0, None, ALU.max))
            c.wait()
            nc.vector.tensor_scalar(has[:, :], keep["deg"][:, :], 0.0, None, ALU.is_gt)
            c.done(nc.vector.reciprocal(keep["inv_deg"][:, :], root[:, :]))
            c.wait()
            dve.sem_inc(deg_cut, 1)
            dve.wait_ge(rooted, 1)
            c.done(nc.vector.reciprocal(keep["dis"][:, :], root[:, :]))
            c.wait()
            nc.vector.tensor_tensor(keep["dis"][:, :], keep["dis"][:, :], has[:, :], ALU.mult).then_inc(dis_ready, 1)
            c.done(nc.vector.memset(wo[:, :, :], 0.0))
            c.wait()
            dve.wait_ge(in_w, 128)
            for h in range(2):
                scale = 1.0 / ((2 * MUL) ** 0.5 * 16.0)
                nc.vector.tensor_scalar(wo[0:MUL, h, 0:MUL], raw[0:MUL, h, :], scale, None, ALU.mult)
                for x in range(3):
                    rows = slice(MUL * (x + 1), MUL * (x + 2))
                    last = nc.vector.tensor_scalar(wo[rows, h, MUL + x:D:3], raw[rows, h, :],
                                                   scale * (3.0 ** 0.5 if h == 0 else 1.0), None, ALU.mult)
            last.then_inc(wo_ready, 1)
            dve.wait_ge(dis_tp, 1)
            nc.vector.tensor_copy(dis_t[:, :], pt[0:NT, 0:P]).then_inc(dis_copied, 1)
            per_turn = 1 + NORM_STEPS + SPLIT_STEPS
            with dve.Fori(0, NG) as g:
                c = Steps(dve, chain, carrier, base=g * per_turn, per_turn=per_turn)
                gate(dve, in_x, 16 * (g + 1), carrier)
                dve.wait_ge(out_ready, g + 1)
                c.done(nc.vector.tensor_tensor(flat(xg[:, :, :]), flat(xg[:, :, :]), px[:, 0:GW], ALU.add))
                c.wait_gated()
                norm_on_vector(nc, dve, c, nb, g, xg, x2g)
                c.wait_gated()
                dve.sem_inc(x2_ready, 1)
                split_on_vector(nc, c, x2g, rest, tabs, g)
                c.wait_gated()
                c.close()

        @block.tensor
        def _(pe):
            pe.wait_ge(dis_ready, 1)
            nc.tensor.transpose(pt[0:NT, 0:P], keep["dis"][:, :], keep["ident"][:, :]).then_inc(dis_tp, 1)
            pe.wait_ge(wo_ready, 1)
            with pe.Fori(0, NG) as g:
                gate(pe, in_msg, 16 * (g + 1), carrier)
                for r in range(GT):
                    for h in range(2):
                        last = nc.tensor.matmul(px[:, r * P:(r + 1) * P], msg[:, r, h * P:(h + 1) * P], wo[:, h, :],
                                                start=h == 0, stop=h == 1, skip_group_check=True)
                last.then_inc(out_ready, 1)
                gate(pe, x2_ready, g + 1, carrier)


def sage(nc, a, d, keep, tabs, AT):
    with ExitStack() as ctx:
        mem = Memory(nc, ctx, "sage")
        sb, ps = mem.sb, mem.ps
        wl, wr = sb("wl", [P, D]), sb("wr", [P, D])
        bias, gamma, beta = sb("bias", [P, D]), sb("gamma", [P, D]), sb("beta", [P, D])
        x2g, x2T, aggT = sb("x2g", [P, GT, D]), sb("x2T", [P, GT, P]), sb("aggT", [P, GT, P])
        f, y = sb("f", [P, GT, D]), sb("y", [P, GT, D])
        nb1, nb2 = NormBuffers(mem, "ln1", LN_EPS), NormBuffers(mem, "ln2", LN_EPS)
        agg, px, pl = ps("agg", [P, 2 * BANK]), ps("px", [P, 2 * BANK]), ps("pl", [P, 2 * BANK])
        carrier, chain, in_w, in_x, agg_ready, agg_copied, xt_ready, xt_copied = mem.sems(
            "carrier chain in_w in_x agg_ready agg_copied xt_ready xt_copied")
        f_ready, p_free, f_sum, gelu_done, x3_ready, stored = mem.sems(
            "f_ready p_free f_sum gelu_done x3_ready stored")
        x2_v, x3_v = tiles_view(d["x2"]), tiles_view(d["x3"])
        mem.clear_at_exit()
        block = ctx.enter_context(nc.Block())

        @block.sync
        def _(sp):
            for dst, src in ((wl, "wlT"), (wr, "wrT")):
                sp.dma_start(dst[:, :], a[src]).then_inc(in_w, 16)
            for dst, src in ((bias, "bl"), (gamma, "gamma"), (beta, "beta")):
                sp.dma_start(dst[:, :], a[src].to_broadcast([P, D])).then_inc(in_w, 16)
            with sp.Fori(0, NG) as g:
                sp.dma_start(x2g[:, :, :], x2_v[:, bass.ds(g * GT, GT), :]).then_inc(in_x, 16)
                sp.wait_ge(x3_ready, g + 1)
                sp.dma_start(x3_v[:, bass.ds(g * GT, GT), :], y[:, :, :]).then_inc(stored, 16)
                gate(sp, stored, 16 * (g + 1), carrier)

        @block.scalar
        def _(act):
            with act.Fori(0, NG) as g:
                act.wait_ge(xt_ready, g + 1)
                nc.scalar.copy(flat(x2T[:, :, :]), px[:, 0:GW]).then_inc(xt_copied, 1)
                act.wait_ge(agg_ready, g + 1)
                nc.scalar.copy(flat(aggT[:, :, :]).rearrange("p (h c) -> p h c", h=2), halves(agg)
                               ).then_inc(agg_copied, 1)
                act.wait_ge(f_sum, g + 1)
                nc.scalar.activation(f[:, :, :], f[:, :, :], ACT.Gelu).then_inc(gelu_done, 1)
                norm_on_scalar(nc, act, nb1, g)
                norm_on_scalar(nc, act, nb2, g)

        @block.vector
        def _(dve):
            dve.wait_ge(in_w, 80)
            dve.sem_inc(p_free, 1)
            per_turn = 1 + NORM_STEPS + 3 + NORM_STEPS

            def over_tiles(v):
                return v[:, :].rearrange("p (o f) -> p o f", o=1).to_broadcast([P, GT, D])

            with dve.Fori(0, NG) as g:
                c = Steps(dve, chain, carrier, base=g * per_turn, per_turn=per_turn)
                dve.wait_ge(f_ready, g + 1)
                c.done(nc.vector.tensor_tensor(f[:, :, :], px[:, 0:GW].rearrange("p (t f) -> p t f", f=D),
                                               over_tiles(bias), ALU.add))
                c.wait_gated()
                for r in range(GT):
                    last = nc.vector.scalar_tensor_tensor(f[:, r, :], pl[:, r * P:(r + 1) * P],
                                                          keep["inv_deg"][:, bass.ds(g * GT + r, 1)], f[:, r, :],
                                                          ALU.mult, ALU.add)
                last.then_inc(f_sum, 1)
                gate(dve, gelu_done, g + 1, carrier)
                dve.sem_inc(p_free, 1)
                norm_on_vector(nc, dve, c, nb1, g, f, y)
                c.wait()
                c.done(nc.vector.tensor_tensor(y[:, :, :], y[:, :, :], over_tiles(gamma), ALU.mult))
                c.wait()
                c.done(nc.vector.tensor_tensor(y[:, :, :], y[:, :, :], over_tiles(beta), ALU.add))
                c.wait()
                c.done(nc.vector.scalar_tensor_tensor(flat(f[:, :, :]), flat(x2g[:, :, :]), 2.0, flat(y[:, :, :]),
                                                      ALU.mult, ALU.add))
                c.wait_gated()
                norm_on_vector(nc, dve, c, nb2, g, f, y)
                c.wait_gated()
                c.close()
                dve.sem_inc(x3_ready, 1)

        @block.tensor
        def _(pe):
            pe.wait_ge(in_w, 80)
            with pe.Fori(0, NG) as g:
                aggregate(nc, agg, tabs, AT, g).then_inc(agg_ready, 1)
                gate(pe, in_x, 16 * (g + 1), carrier)
                gate(pe, p_free, g + 1, carrier)
                for r in range(GT):
                    last = nc.tensor.transpose(px[:, r * P:(r + 1) * P], x2g[:, r, :], keep["ident"][:, :])
                last.then_inc(xt_ready, 1)
                gate(pe, agg_copied, g + 1, carrier)
                for r in range(GT):
                    nc.tensor.matmul(pl[:, r * P:(r + 1) * P], aggT[:, r, :], wl[:, :], start=True, stop=True,
                                     skip_group_check=True)
                gate(pe, xt_copied, g + 1, carrier)
                for r in range(GT):
                    last = nc.tensor.matmul(px[:, r * P:(r + 1) * P], x2T[:, r, :], wr[:, :], start=True, stop=True,
                                            skip_group_check=True)
                last.then_inc(f_ready, 1)


def project(nc, a, d, keep, tabs):
    with ExitStack() as ctx:
        mem = Memory(nc, ctx, "proj")
        sb, ps = mem.sb, mem.ps
        w = sb("w", [P, D])
        xg, xT, hg, rest = (sb(n, [P, GT, D]) for n in ("xg", "xT", "hg", "rest"))
        px, ph = ps("px", [P, 2 * BANK]), ps("ph", [P, 2 * BANK])
        carrier, chain, in_w, in_x, xt_ready, xt_copied, h_ready, h_split = mem.sems(
            "carrier chain in_w in_x xt_ready xt_copied h_ready h_split")
        x3_v = tiles_view(d["x3"])
        mem.clear_at_exit()
        block = ctx.enter_context(nc.Block())

        @block.sync
        def _(sp):
            sp.dma_start(w[:, :], a["g1"]).then_inc(in_w, 16)
            with sp.Fori(0, NG) as g:
                sp.dma_start(xg[:, :, :], x3_v[:, bass.ds(g * GT, GT), :]).then_inc(in_x, 16)
                gate(sp, xt_ready, g + 1, carrier)

        @block.scalar
        def _(act):
            with act.Fori(0, NG) as g:
                act.wait_ge(xt_ready, g + 1)
                nc.scalar.copy(flat(xT[:, :, :]), px[:, 0:GW]).then_inc(xt_copied, 1)

        @block.vector
        def _(dve):
            per_turn = 1 + SPLIT_STEPS
            dve.sem_inc(h_split, 1)
            with dve.Fori(0, NG) as g:
                c = Steps(dve, chain, carrier, base=g * per_turn, per_turn=per_turn)
                dve.wait_ge(h_ready, g + 1)
                scale_tiles(nc, c, hg, ph, keep["dis"], g)
                c.wait()
                split_on_vector(nc, c, hg, rest, tabs, g)
                c.wait_gated()
                c.close()
                dve.sem_inc(h_split, 1)

        @block.tensor
        def _(pe):
            pe.wait_ge(in_w, 16)
            with pe.Fori(0, NG) as g:
                gate(pe, in_x, 16 * (g + 1), carrier)
                for r in range(GT):
                    last = nc.tensor.transpose(px[:, r * P:(r + 1) * P], xg[:, r, :], keep["ident"][:, :])
                last.then_inc(xt_ready, 1)
                gate(pe, xt_copied, g + 1, carrier)
                gate(pe, h_split, g + 1, carrier)
                for r in range(GT):
                    last = nc.tensor.matmul(ph[:, r * P:(r + 1) * P], xT[:, r, :], w[:, :], start=True, stop=True,
                                            skip_group_check=True)
                last.then_inc(h_ready, 1)


def scale_tiles(nc, c, dst, src, factor, g):
    for r in range(GT):
        last = nc.vector.tensor_scalar(dst[:, r, :], src[:, r * P:(r + 1) * P],
                                       factor[:, bass.ds(g * GT + r, 1)], None, ALU.mult)
    c.done(last)


def gcn(nc, a, d, keep, layer, tabs, next_tabs, AT, out):
    final = next_tabs is None
    with ExitStack() as ctx:
        mem = Memory(nc, ctx, f"gcn{layer}")
        sb, ps = mem.sb, mem.ps
        w, b = sb("w", [P, D]), sb("b", [P, 1])
        row, hT, hg = sb("row", [P, GW]), sb("hT", [P, GT, P]), sb("hg", [P, GT, D])
        rest = sb("rest", [P, GT, D])
        nb = NormBuffers(mem, "ln", LN_EPS) if final else None
        agg, ph = ps("agg", [P, 2 * BANK]), ps("ph", [P, 2 * BANK])
        carrier, chain, in_w, in_row, in_x, agg_ready, agg_scaled, ht_ready, h_ready, done, out_ready, stored = mem.sems(
            "carrier chain in_w in_row in_x agg_ready agg_scaled ht_ready h_ready done out_ready stored")
        x3_v, out_v = tiles_view(d["x3"]), tiles_view(out)
        mem.clear_at_exit()
        block = ctx.enter_context(nc.Block())

        @block.sync
        def _(sp):
            if not final:
                sp.dma_start(w[:, :], a[f"g{layer + 1}"]).then_inc(in_w, 16)
            sp.dma_start(b[:, :], a[f"gb{layer}"]).then_inc(in_w, 16)
            with sp.Fori(0, NG) as g:
                sp.dma_start(row[:, :], d["dis"][:, bass.ds(g * GW, GW)].to_broadcast([P, GW])).then_inc(in_row, 16)
                if final:
                    sp.dma_start(hg[:, :, :], x3_v[:, bass.ds(g * GT, GT), :]).then_inc(in_x, 16)
                    sp.wait_ge(out_ready, g + 1)
                    sp.dma_start(out_v[:, bass.ds(g * GT, GT), :], rest[:, :, :]).then_inc(stored, 16)
                    gate(sp, stored, 16 * (g + 1), carrier)
                else:
                    gate(sp, agg_scaled, g + 1, carrier)

        @block.scalar
        def _(act):
            act.wait_ge(in_w, 16 if final else 32)
            with act.Fori(0, NG) as g:
                act.wait_ge(agg_scaled, g + 1)
                nc.scalar.activation(flat(hT[:, :, :]), flat(hT[:, :, :]), ACT.Identity if final else ACT.Relu,
                                     bias=b[:, 0:1]).then_inc(ht_ready, 1)
                if final:
                    norm_on_scalar(nc, act, nb, g)

        @block.vector
        def _(dve):
            per_turn = 1 + NORM_STEPS if final else 1 + SPLIT_STEPS
            dve.sem_inc(done, 1)
            with dve.Fori(0, NG) as g:
                c = Steps(dve, chain, carrier, base=g * per_turn, per_turn=per_turn)
                gate(dve, in_row, 16 * (g + 1), carrier)
                dve.wait_ge(agg_ready, g + 1)
                nc.vector.tensor_tensor(flat(hT[:, :, :]).rearrange("p (h c) -> p h c", h=2), halves(agg),
                                        row[:, :].rearrange("p (h c) -> p h c", h=2), ALU.mult).then_inc(agg_scaled, 1)
                if final:
                    gate(dve, in_x, 16 * (g + 1), carrier)
                    dve.wait_ge(h_ready, g + 1)
                    c.done(nc.vector.tensor_tensor(flat(hg[:, :, :]), flat(hg[:, :, :]), ph[:, 0:GW], ALU.add))
                    c.wait_gated()
                    norm_on_vector(nc, dve, c, nb, g, hg, rest)
                    c.wait_gated()
                    dve.sem_inc(out_ready, 1)
                else:
                    dve.wait_ge(h_ready, g + 1)
                    scale_tiles(nc, c, hg, ph, keep["dis"], g)
                    c.wait()
                    split_on_vector(nc, c, hg, rest, next_tabs, g)
                    c.wait_gated()
                c.close()
                dve.sem_inc(done, 1)

        @block.tensor
        def _(pe):
            pe.wait_ge(in_w, 16 if final else 32)
            with pe.Fori(0, NG) as g:
                aggregate(nc, agg, tabs, AT, g).then_inc(agg_ready, 1)
                gate(pe, ht_ready, g + 1, carrier)
                gate(pe, done, g + 1, carrier)
                for r in range(GT):
                    if final:
                        last = nc.tensor.transpose(ph[:, r * P:(r + 1) * P], hT[:, r, :], keep["ident"][:, :])
                    else:
                        last = nc.tensor.matmul(ph[:, r * P:(r + 1) * P], hT[:, r, :], w[:, :], start=True,
                                                stop=True, skip_group_check=True)
                last.then_inc(h_ready, 1)


def build(nc, a, out):
    def dram(name, shape, dt=F32):
        return nc.dram_tensor(name, shape, dt, kind="Internal").ap()

    basis = dram("basis_d", (NBAS, EP))
    d = {
        "z": dram("z_d", (P, NT, ZW)), "es_row": dram("es_row_d", (1, NP)),
        "basis": basis, "basis_pk": basis.rearrange("k (s e) -> (k s) e", e=SEG),
        "unit": dram("unit_d", (P, NC, 3)), "rows": dram("rows_d", (2, NP)), "x1": dram("x1_d", (NP, D)),
        "table": dram("table_d", (NP, D)), "msg": dram("msg_d", (P, NT, 2, P)), "x2": dram("x2_d", (NP, D)),
        "x3": dram("x3_d", (NP, D)), "dis": dram("dis_d", (1, NP)),
    }
    with ExitStack() as ctx:
        def sb(name, shape, dt=F32):
            return ctx.enter_context(nc.sbuf_tensor(name, shape, dt))

        keep = {
            "rng": sb("rng", [1, 3 * NR], I32), "es_min": sb("es_min", [P, 1]), "es_max": sb("es_max", [P, NT]),
            "deg": sb("deg", [P, NT]), "dis": sb("dis", [P, NT]), "inv_deg": sb("inv_deg", [P, NT]),
            "ident": sb("ident", [P, P]), "ident_bf": sb("ident_bf", [P, P], BF16),
        }
        prepare(nc, a, d, keep)
        AT = sb("AT", [P, NT, NP], BF16)
        build_counts(nc, a, d, keep, AT)
        attention(nc, a, d, keep, AT)
        edge_messages(nc, a, d, keep)
        tabs = [[sb(f"tab0{i}", [P, NT, D], BF16) for i in range(3)]]
        update_messages(nc, a, d, keep, tabs[0])
        sage(nc, a, d, keep, tabs[0], AT)
        project(nc, a, d, keep, tabs[0])
        tabs.append([sb(f"tab1{i}", [P, NT, D], BF16) for i in range(3)])
        gcn(nc, a, d, keep, 1, tabs[0], tabs[1], AT, out)
        gcn(nc, a, d, keep, 2, tabs[1], tabs[0], AT, out)
        gcn(nc, a, d, keep, 3, tabs[0], None, AT, out)


_OUT = (NP, D)


def kernel(**inputs):
    import numpy as _np
    import concourse.bacc as _bacc
    from concourse import mybir as _mybir
    from concourse.bass_utils import run_bass_kernel_spmd as _run

    v = {k: _np.asarray(x) for k, x in inputs.items()}

    def padded(x, rows, fill=0):
        y = _np.full((rows,) + x.shape[1:], fill, x.dtype)
        y[:x.shape[0]] = x
        return y

    def by_chunk(x):
        return _np.ascontiguousarray(_np.moveaxis(x.reshape((NC, P) + x.shape[1:]), 1, 0))

    x = padded(v["x"], NP)
    dst = padded(v["dst"], EP, NP - 1)
    col = lambda w: w.reshape(-1, 1)
    row = lambda w: w.reshape(1, -1)
    arrays = {
        "x": x, "xT": x.T, "src": by_chunk(padded(v["src"], EP)), "dst": by_chunk(dst),
        "dst_blk": dst.reshape(RP, 2 * BLK), "vec": by_chunk(padded(v["edge_attr_3"], EP)),
        "radius": padded(v["edge_weight"], EP).reshape(P // NBAS, SEG),
        "w0": v["L0_gnn_W"], "w0T": v["L0_gnn_W"].T, "a_s": col(v["L0_gnn_a_s"]), "a_d": col(v["L0_gnn_a_d"]),
        "up0": v["L1_gnn_W_up0"], "up1": v["L1_gnn_W_up1"],
        "mw0": v["L1_gnn_mlp_w0"], "mb0": col(v["L1_gnn_mlp_b0"]), "mw1": v["L1_gnn_mlp_w1"],
        "mb1": col(v["L1_gnn_mlp_b1"]), "mw2": v["L1_gnn_mlp_w2"], "mb2": row(v["L1_gnn_mlp_b2"]),
        "out0": v["L1_gnn_W_out0"], "out1": v["L1_gnn_W_out1"],
        "wlT": v["L2_gnn_W_l"].T, "bl": row(v["L2_gnn_b_l"]), "wrT": v["L2_gnn_W_r"].T,
        "gamma": row(v["L2_gnn_ln_gamma"]), "beta": row(v["L2_gnn_ln_beta"]),
        "g1": v["L3_gnn_W1"], "g2": v["L3_gnn_W2"], "g3": v["L3_gnn_W3"],
        "gb1": col(v["L3_gnn_b1"]), "gb2": col(v["L3_gnn_b2"]), "gb3": col(v["L3_gnn_b3"]),
    }
    arrays = {f"in_{k}": _np.ascontiguousarray(w) for k, w in arrays.items()}
    nc = _bacc.Bacc("TRN2", target_bir_lowering=False, num_devices=1)
    a = {k[3:]: nc.dram_tensor(k, w.shape, _mybir.dt.from_np(w.dtype), kind="ExternalInput").ap()
         for k, w in arrays.items()}
    out = nc.dram_tensor("out", _OUT, F32, kind="ExternalOutput").ap()
    build(nc, a, out)
    r = _run(nc, [arrays], core_ids=[0])
    return _np.asarray(r.results[0]["out"])[:N]
```
